# Optimizing a Trainium2 kernel written in Bass

```python
import numpy as np
import jax
import jax.numpy as jnp

def _softmax(x, axis=-1):
    return jax.nn.softmax(x, axis=axis)

def _gelu(x):
    return jax.nn.gelu(x, approximate=True)

def _silu(x):
    return jax.nn.silu(x)

def _sigmoid(x):
    return jax.nn.sigmoid(x)

def _layernorm(x, axis=-1, eps=1e-05):
    m = jnp.mean(x, axis=axis, keepdims=True)
    v = jnp.var(x, axis=axis, keepdims=True)
    return (x - m) / jnp.sqrt(v + eps)

def _scatter_add(tgt, idx, src, axis=0):
    return tgt.at[idx].add(src)

def _segment_sum(src, seg, n):
    return jax.ops.segment_sum(src, seg, n)
kernel_name = 'mk_dlrm_tower_d1_rec_r8_fe93c4'

def setup_inputs(seed: int=0):
    np.random.seed(seed)
    _w = jnp.asarray

    def _rec_inputs():
        import jax
        import jax.numpy as jnp
        _tk = jax.random.key(seed)
        dense_ctx = jax.random.normal(jax.random.fold_in(_tk, 190), (2048, 16), jnp.float32)
        ids = jnp.stack([jax.random.randint(jax.random.fold_in(_tk, 200 + f), (2048,), 0, v, jnp.int32) for f, v in enumerate([1000, 1250, 1000, 1000, 12500, 1250, 1000, 1000, 12500, 125000, 12500, 1000, 1000, 12500, 12500, 12500, 1250, 12500, 1000, 12500, 1000, 1000, 1000, 1000, 12500, 1000, 1000])], axis=1)
        tbl_0 = 0.05 * jax.random.normal(jax.random.fold_in(_tk, 500 + 0), (1000, 128), jnp.float32)
        tbl_1 = 0.05 * jax.random.normal(jax.random.fold_in(_tk, 500 + 1), (1250, 128), jnp.float32)
        tbl_2 = 0.05 * jax.random.normal(jax.random.fold_in(_tk, 500 + 2), (1000, 128), jnp.float32)
        tbl_3 = 0.05 * jax.random.normal(jax.random.fold_in(_tk, 500 + 3), (1000, 128), jnp.float32)
        tbl_4 = 0.05 * jax.random.normal(jax.random.fold_in(_tk, 500 + 4), (12500, 128), jnp.float32)
        tbl_5 = 0.05 * jax.random.normal(jax.random.fold_in(_tk, 500 + 5), (1250, 128), jnp.float32)
        tbl_6 = 0.05 * jax.random.normal(jax.random.fold_in(_tk, 500 + 6), (1000, 128), jnp.float32)
        tbl_7 = 0.05 * jax.random.normal(jax.random.fold_in(_tk, 500 + 7), (1000, 128), jnp.float32)
        tbl_8 = 0.05 * jax.random.normal(jax.random.fold_in(_tk, 500 + 8), (12500, 128), jnp.float32)
        tbl_9 = 0.05 * jax.random.normal(jax.random.fold_in(_tk, 500 + 9), (125000, 128), jnp.float32)
        tbl_10 = 0.05 * jax.random.normal(jax.random.fold_in(_tk, 500 + 10), (12500, 128), jnp.float32)
        tbl_11 = 0.05 * jax.random.normal(jax.random.fold_in(_tk, 500 + 11), (1000, 128), jnp.float32)
        tbl_12 = 0.05 * jax.random.normal(jax.random.fold_in(_tk, 500 + 12), (1000, 128), jnp.float32)
        tbl_13 = 0.05 * jax.random.normal(jax.random.fold_in(_tk, 500 + 13), (12500, 128), jnp.float32)
        tbl_14 = 0.05 * jax.random.normal(jax.random.fold_in(_tk, 500 + 14), (12500, 128), jnp.float32)
        tbl_15 = 0.05 * jax.random.normal(jax.random.fold_in(_tk, 500 + 15), (12500, 128), jnp.float32)
        tbl_16 = 0.05 * jax.random.normal(jax.random.fold_in(_tk, 500 + 16), (1250, 128), jnp.float32)
        tbl_17 = 0.05 * jax.random.normal(jax.random.fold_in(_tk, 500 + 17), (12500, 128), jnp.float32)
        tbl_18 = 0.05 * jax.random.normal(jax.random.fold_in(_tk, 500 + 18), (1000, 128), jnp.float32)
        tbl_19 = 0.05 * jax.random.normal(jax.random.fold_in(_tk, 500 + 19), (12500, 128), jnp.float32)
        tbl_20 = 0.05 * jax.random.normal(jax.random.fold_in(_tk, 500 + 20), (1000, 128), jnp.float32)
        tbl_21 = 0.05 * jax.random.normal(jax.random.fold_in(_tk, 500 + 21), (1000, 128), jnp.float32)
        tbl_22 = 0.05 * jax.random.normal(jax.random.fold_in(_tk, 500 + 22), (1000, 128), jnp.float32)
        tbl_23 = 0.05 * jax.random.normal(jax.random.fold_in(_tk, 500 + 23), (1000, 128), jnp.float32)
        tbl_24 = 0.05 * jax.random.normal(jax.random.fold_in(_tk, 500 + 24), (12500, 128), jnp.float32)
        tbl_25 = 0.05 * jax.random.normal(jax.random.fold_in(_tk, 500 + 25), (1000, 128), jnp.float32)
        tbl_26 = 0.05 * jax.random.normal(jax.random.fold_in(_tk, 500 + 26), (1000, 128), jnp.float32)
        _rk = jax.random.fold_in(_tk, 7)
        W_top1 = 0.0521996 * jax.random.normal(jax.random.fold_in(_tk, 801), (367, 512), jnp.float32)
        W_top2 = 0.0441942 * jax.random.normal(jax.random.fold_in(_tk, 802), (512, 256), jnp.float32)
        W_top3 = 0.0625 * jax.random.normal(jax.random.fold_in(_tk, 803), (256, 1), jnp.float32)
        b_top1 = jnp.zeros((512,), jnp.float32)
        b_top2 = jnp.zeros((256,), jnp.float32)
        return (dense_ctx, ids, tbl_0, tbl_1, tbl_2, tbl_3, tbl_4, tbl_5, tbl_6, tbl_7, tbl_8, tbl_9, tbl_10, tbl_11, tbl_12, tbl_13, tbl_14, tbl_15, tbl_16, tbl_17, tbl_18, tbl_19, tbl_20, tbl_21, tbl_22, tbl_23, tbl_24, tbl_25, tbl_26, W_top1, b_top1, W_top2, b_top2, W_top3)
    dense_ctx, ids, tbl_0, tbl_1, tbl_2, tbl_3, tbl_4, tbl_5, tbl_6, tbl_7, tbl_8, tbl_9, tbl_10, tbl_11, tbl_12, tbl_13, tbl_14, tbl_15, tbl_16, tbl_17, tbl_18, tbl_19, tbl_20, tbl_21, tbl_22, tbl_23, tbl_24, tbl_25, tbl_26, W_top1, b_top1, W_top2, b_top2, W_top3 = _rec_inputs()

    def _L0_rec_setup():
        import jax, jax.numpy as jnp
        import numpy as np
        NUM_FEATURES = 27
        EMBED_DIM = 128
        BATCH = 4096
        key = jax.random.key(seed)
        inputs = jax.random.normal(key, (BATCH, NUM_FEATURES, EMBED_DIM), dtype=jnp.float32)
        return {'inputs': inputs}
    _L0_rec_all = _L0_rec_setup()
    _L0_rec_in = {k: v for k, v in _L0_rec_all.items() if k in ()}
    del _L0_rec_all
    return {'dense_ctx': dense_ctx, 'ids': ids, 'tbl_0': tbl_0, 'tbl_1': tbl_1, 'tbl_2': tbl_2, 'tbl_3': tbl_3, 'tbl_4': tbl_4, 'tbl_5': tbl_5, 'tbl_6': tbl_6, 'tbl_7': tbl_7, 'tbl_8': tbl_8, 'tbl_9': tbl_9, 'tbl_10': tbl_10, 'tbl_11': tbl_11, 'tbl_12': tbl_12, 'tbl_13': tbl_13, 'tbl_14': tbl_14, 'tbl_15': tbl_15, 'tbl_16': tbl_16, 'tbl_17': tbl_17, 'tbl_18': tbl_18, 'tbl_19': tbl_19, 'tbl_20': tbl_20, 'tbl_21': tbl_21, 'tbl_22': tbl_22, 'tbl_23': tbl_23, 'tbl_24': tbl_24, 'tbl_25': tbl_25, 'tbl_26': tbl_26, 'W_top1': W_top1, 'b_top1': b_top1, 'W_top2': W_top2, 'b_top2': b_top2, 'W_top3': W_top3}

def reference(dense_ctx, ids, tbl_0, tbl_1, tbl_2, tbl_3, tbl_4, tbl_5, tbl_6, tbl_7, tbl_8, tbl_9, tbl_10, tbl_11, tbl_12, tbl_13, tbl_14, tbl_15, tbl_16, tbl_17, tbl_18, tbl_19, tbl_20, tbl_21, tbl_22, tbl_23, tbl_24, tbl_25, tbl_26, W_top1, b_top1, W_top2, b_top2, W_top3):
    import jax
    import jax.numpy as jnp

    def _L0_rec_ref(inputs):
        import jax, jax.numpy as jnp
        import numpy as np
        NUM_FEATURES = 27
        EMBED_DIM = 128
        BATCH = 4096
        interactions = jnp.einsum('bnd,bmd->bnm', inputs, inputs)
        n = inputs.shape[1]
        i, j = jnp.triu_indices(n, k=1)
        return interactions[:, i, j]
    e = jnp.stack([tbl_0[ids[:, 0]], tbl_1[ids[:, 1]], tbl_2[ids[:, 2]], tbl_3[ids[:, 3]], tbl_4[ids[:, 4]], tbl_5[ids[:, 5]], tbl_6[ids[:, 6]], tbl_7[ids[:, 7]], tbl_8[ids[:, 8]], tbl_9[ids[:, 9]], tbl_10[ids[:, 10]], tbl_11[ids[:, 11]], tbl_12[ids[:, 12]], tbl_13[ids[:, 13]], tbl_14[ids[:, 14]], tbl_15[ids[:, 15]], tbl_16[ids[:, 16]], tbl_17[ids[:, 17]], tbl_18[ids[:, 18]], tbl_19[ids[:, 19]], tbl_20[ids[:, 20]], tbl_21[ids[:, 21]], tbl_22[ids[:, 22]], tbl_23[ids[:, 23]], tbl_24[ids[:, 24]], tbl_25[ids[:, 25]], tbl_26[ids[:, 26]]], axis=1)
    z = _L0_rec_ref(e)
    z = z.reshape(z.shape[0], -1)
    h = jnp.concatenate([z, dense_ctx], axis=1)
    h = jnp.maximum(h @ W_top1 + b_top1, 0.0)
    h = jnp.maximum(h @ W_top2 + b_top2, 0.0)
    y = h @ W_top3
    return y

_drawn_inputs = setup_inputs


def setup_inputs(seed=0):
    import zlib

    import numpy as np

    out = dict(_drawn_inputs(seed))
    spreads = {'b_top1': (0.0, 0.1), 'b_top2': (0.0, 0.1)}
    factors = {}
    for name, (base, spread) in spreads.items():
        noise = np.random.default_rng([zlib.crc32(name.encode()), seed]).standard_normal(out[name].shape)
        drawn = base * np.exp(spread * noise) if base else spread * noise
        out[name] = jnp.asarray(drawn.astype(out[name].dtype))
    for name, factor in factors.items():
        out[name] = (out[name] * factor).astype(out[name].dtype)
    return out
```

```python
from contextlib import ExitStack

import numpy as np

import concourse.bass as bass
from concourse import mybir

F32 = mybir.dt.float32
F32R = mybir.dt.float32r
I32 = mybir.dt.int32
ALU = mybir.AluOpType
ACT = mybir.ActivationFunctionType

B = 2048
F = 27
D = 128
CTX = 16
H1, H2 = 512, 256
P = 128
MT = 256
NM = B // MT
HALF = MT // P
FS = 32
FM = 28
J = FM // 4
STAGES = 3

ONE_HOT = (0, 2, 3, 6, 7, 11, 12, 18)
ROWS = 1000
TP = 125
TC = ROWS // TP
GATHER = tuple(f for f in range(F) if f not in ONE_HOT)
NX = len(ONE_HOT)
OH_SLOTS = 8


def pairs(features):
    return [features[i:i + 2] for i in range(0, len(features), 2)]


OH_UNITS = pairs(ONE_HOT)
GA_UNITS = pairs(GATHER)
NI = len(OH_UNITS)
STEPS = [(u, list(range(2 * u, 2 * u + 2))) for u in range(NI)]
TAIL_UNITS = list(range(2 * NI, len(GA_UNITS)))
SEQ = []
for _u, _g in STEPS:
    SEQ.append(("oh", _u))
    SEQ += [("ga", _j) for _j in _g]
SEQ += [("ga", _j) for _j in TAIL_UNITS]
NU = len(SEQ)
NJ = len(GA_UNITS)
PARTS = (range(0, NJ // 2), range(NJ // 2, NJ))
assert NU % 2 == 0 and NI % 2 == 0 and NI >= 4

CH_OF = [len(u) * TC for u in OH_UNITS]
CH_AT = [sum(CH_OF[:u]) for u in range(NI + 1)]
NCH = CH_AT[NI]
assert NCH % OH_SLOTS == 0
NB = 8
BS = MT // NB
NG = BS // 4
NL = 7


def build(nc, ids, ids_t, ctx_t, tables, w1z, b1, w2, b2, w3, out):
    ctx = ExitStack()
    with ctx:
        def sb(name, shape, dt=F32):
            return ctx.enter_context(nc.sbuf_tensor(name, shape, dt))

        def sem(name):
            return ctx.enter_context(nc.semaphore(name))

        ident = sb("ident", [P, P])
        row_of = sb("row_of", [P, TC])
        sel = sb("sel", [NX, NX, P], F32R)
        ids_rows = [sb(f"ids_rows{i}", [P, HALF, F], I32) for i in range(2)]
        ids_f = sb("ids_f", [NX, B], F32R)
        tab_hi = sb("tab_hi", [P, NX, TC, D], F32R)
        tab_lo = sb("tab_lo", [P, NX, TC, D], F32R)
        one_hot = sb("one_hot", [P, OH_SLOTS, MT], F32R)
        rows = sb("rows", [P, len(GATHER), HALF, D])
        x_hi = sb("x_hi", [P, MT * FS], F32R)
        x_lo = sb("x_lo", [P, MT * FS], F32R)
        z = sb("z", [P, J, MT])
        w1_sb = sb("w1_sb", [P, J, H1])
        w2_sb = sb("w2_sb", [P, H1 // P, H2])
        w3_sb = sb("w3_sb", [P, H2 // P])
        b1_sb = sb("b1_sb", [P, H1 // P])
        b2_sb = sb("b2_sb", [P, H2 // P])
        h1 = sb("h1", [P, H1 // P, MT])
        h2 = sb("h2", [P, H2 // P, MT])
        y = sb("y", [1, MT])
        ids_ps = ctx.enter_context(nc.psum_tensor("ids_ps", [P, 2, 512], F32))
        x_ps = ctx.enter_context(nc.psum_tensor("x_ps", [P, 2, 512], F32))
        g_ps = ctx.enter_context(nc.psum_tensor("g_ps", [P, 4, 512], F32))

        ids_loaded = [sem(f"ids_loaded{i}") for i in range(2)]
        idsr_loaded = sem("idsr_loaded")
        tab_loaded = [sem(f"tab_loaded{i}") for i in range(STAGES)]
        tab_hi_done = sem("tab_hi_done")
        tab_lo_done = sem("tab_lo_done")
        w_loaded = sem("w_loaded")
        ident_zero = sem("ident_zero")
        ident_done = sem("ident_done")
        row_done = sem("row_done")
        const_done = sem("const_done")
        pads_done = sem("pads_done")
        ids_bcast = sem("ids_bcast")
        oh_ready = sem("oh_ready")
        oh_used = sem("oh_used")
        gathered = [sem(f"gathered{j}") for j in range(len(GA_UNITS))]
        transposed = sem("transposed")
        hi_done = sem("hi_done")
        lo_done = sem("lo_done")
        gram_ready = sem("gram_ready")
        z_act = sem("z_act")
        z_dve = sem("z_dve")
        ctx_loaded = sem("ctx_loaded")
        l_ready = sem("l_ready")
        l_out = sem("l_out")
        y_stored = sem("y_stored")

        w1_flat = w1_sb[:, :, :].rearrange("p j k -> p (j k)")
        stage_ids = w1_flat[0:NX, 0:B].bitcast(I32)
        stage = [w1_flat[0:TP, i * TC * D:(i + 1) * TC * D] for i in range(STAGES)]
        assert STAGES * TC * D <= J * H1

        xh = x_hi[:, :].rearrange("p (b f) -> p b f", f=FS)
        xl = x_lo[:, :].rearrange("p (b f) -> p b f", f=FS)

        def span(features):
            a, b = features[0], features[-1]
            return slice(a, b + 1, max(b - a, 1))

        def unit_features(unit):
            kind, n = unit
            return OH_UNITS[n] if kind == "oh" else GA_UNITS[n]

        def x_bank(v, n):
            return x_ps[:, v % 2, 0:n * MT]

        def macro_tiles(engine, body):
            body(0, True, False)
            with engine.Fori(1, NM - 1) as t:
                body(t, False, False)
            body(NM - 1, False, True)

        def copy_blocks(copy, b, quadrants, signal):
            src = g_ps[:, 2 * (b % 2):2 * (b % 2) + 2, 0:4 * 4 * FM].rearrange("p a (g s j q) -> p a g s j q", g=4, s=4, q=4)
            dst = z[:, :, b * BS:(b + 1) * BS].rearrange("p j (a g s) -> p a g s j", g=4, s=4)
            for s in quadrants:
                for q in range(4):
                    nj = J - 1 if q == 3 else J
                    for a in range(NG // 4):
                        last = copy(dst[32 * q:32 * q + F, a, :, s, 0:nj],
                                    src[32 * s:32 * s + F, a, :, s, 0:nj, q])
            last.then_inc(signal, 1)

        block = ctx.enter_context(nc.Block())

        @block.sync
        def _(sp):
            def load_ids(t, part):
                sp.dma_start(ids_rows[part][:, :, :],
                             ids.rearrange("(c p) f -> p c f", p=P)[:, bass.ds(t * HALF, HALF), :]).then_inc(ids_loaded[part], 16)

            for part in range(2):
                load_ids(0, part)
            for i, f in enumerate(ONE_HOT):
                sp.dma_start(stage_ids[i:i + 1, 0:B], ids_t[f:f + 1, :]).then_inc(idsr_loaded, 16)
            sp.wait_ge(const_done, 2)
            for i in range(NX):
                if i >= STAGES:
                    sp.wait_ge(tab_lo_done, i - STAGES + 1)
                sp.dma_start(stage[i % STAGES],
                             tables[ONE_HOT[i]].rearrange("(p c) d -> p (c d)", c=TC)).then_inc(tab_loaded[i % STAGES], 16)
            sp.wait_ge(tab_lo_done, NX)
            sp.dma_start(w1_sb[:, :, :], w1z.rearrange("p j k -> p (j k)")).then_inc(w_loaded, 16)
            sp.dma_start(w2_sb[:, :, :], w2.rearrange("(k p) n -> p k n", p=P)).then_inc(w_loaded, 16)
            with nc.allow_non_contiguous_dma(reason="biases and the last layer's weights, once"):
                sp.dma_start(w3_sb[:, :], w3.rearrange("(k p) n -> p (k n)", p=P)).then_inc(w_loaded, 16)
                sp.dma_start(b1_sb[:, :], b1.rearrange("(k p) -> p k", p=P)).then_inc(w_loaded, 16)
                sp.dma_start(b2_sb[:, :], b2.rearrange("(k p) -> p k", p=P)).then_inc(w_loaded, 16)

            def body(t, first, last):
                for part, units in enumerate(PARTS):
                    for j in units:
                        sp.wait_ge(gathered[j], 16 * HALF * len(GA_UNITS[j]) * (t + 1))
                        sp.nop(nofuse=True)
                    load_ids(t + 1, part)

            body(0, True, False)
            with sp.Fori(1, NM - 1) as t:
                body(t, False, False)

        @block.gpsimd
        def _(pool):
            pool.memset(ident[:, :], 0.0).then_inc(ident_zero, 1)
            pool.wait_ge(ident_zero, 1)
            pool.affine_select(out=ident[:, :], in_=ident[:, :], compare_op=ALU.not_equal, fill=1.0,
                               base=0, pattern=[[-1, P]], channel_multiplier=1).then_inc(ident_done, 1)
            pool.iota(row_of[:, :], pattern=[[1, TC]], base=0, channel_multiplier=TC,
                      allow_small_or_imprecise_dtypes=True).then_inc(row_done, 1)

            def body(t, first, last):
                for j, unit in enumerate(GA_UNITS):
                    part = int(j in PARTS[1])
                    if j in (PARTS[0][0], PARTS[1][0]):
                        pool.wait_ge(ids_loaded[part], 16 * t + 16)
                        pool.nop(nofuse=True)
                    if not first:
                        pool.wait_ge(transposed, NJ * (t - 1) + j + 1)
                        pool.nop(nofuse=True)
                    for f in unit:
                        for h in range(HALF):
                            pool.indirect_dma_start(
                                out=rows[:, GATHER.index(f), h, :], out_offset=None, in_=tables[f][:, :],
                                in_offset=bass.IndirectOffsetOnAxis(
                                    ap=ids_rows[part][:, h, f:f + 1], axis=0),
                            ).then_inc(gathered[j], 16)

            macro_tiles(pool, body)

        @block.vector
        def _(dve):
            dve.memset(z[:, :, :], 0.0).then_inc(pads_done, 1)
            dve.memset(xh[:, :, F:FS].bitcast(F32), 0.0)
            dve.memset(xl[:, :, F:FS].bitcast(F32), 0.0).then_inc(pads_done, 1)
            dve.wait_ge(ident_done, 1)
            dve.tensor_copy(sel[:, :, :], ident[0:NX, 0:NX].unsqueeze(2).to_broadcast([NX, NX, P])).then_inc(const_done, 1)
            dve.wait_ge(idsr_loaded, 16 * NX)
            dve.tensor_copy(ids_f[:, :], stage_ids).then_inc(const_done, 1)
            for i in range(NX):
                dve.wait_ge(tab_hi_done, i + 1)
                dve.tensor_tensor(tab_lo[0:TP, i, :, :].rearrange("p c d -> p (c d)"), stage[i % STAGES],
                                  tab_hi[0:TP, i, :, :].rearrange("p c d -> p (c d)").bitcast(F32),
                                  ALU.subtract).then_inc(tab_lo_done, 1)
            dve.wait_ge(row_done, 1)

            def make_one_hots(t, u, part=None, parts=1):
                n = CH_OF[u] // parts
                todo = range(CH_OF[u]) if part is None else range(part * n, part * n + n)
                for c in todo:
                    at = CH_AT[u] + c
                    if c == todo[0]:
                        dve.wait_ge(ids_bcast, NI * t + u + 1)
                    if not (isinstance(t, int) and t == 0 and at < OH_SLOTS):
                        dve.wait_ge(oh_used, NCH * t + at - OH_SLOTS + 1)
                    dve.tensor_scalar(one_hot[0:TP, at % OH_SLOTS, :],
                                      ids_ps[0:TP, u % 2, (c // TC) * MT:(c // TC + 1) * MT],
                                      row_of[0:TP, c % TC:c % TC + 1], None, ALU.is_equal).then_inc(oh_ready, 1)

            def low_part(t, v):
                features = unit_features(SEQ[v])
                dve.wait_ge(hi_done, NU * t + v + 1)
                dve.tensor_tensor(xl[:, :, span(features)],
                                  x_bank(v, len(features)).rearrange("p (f b) -> p b f", b=MT),
                                  xh[:, :, span(features)].bitcast(F32), ALU.subtract).then_inc(lo_done, 1)

            def body(t, first, last):
                make_one_hots(t, 0, 1, 2)
                v = 0
                for u, units in STEPS:
                    ahead = u + 1 < NI
                    if ahead:
                        make_one_hots(t, u + 1, 0, 2)
                    low_part(t, v)
                    for k in range(len(units) - 1):
                        low_part(t, v + 1 + k)
                    if ahead:
                        make_one_hots(t, u + 1, 1, 2)
                    low_part(t, v + len(units))
                    v += 1 + len(units)
                for v in range(v, NU):
                    low_part(t, v)
                for b in range(NB):
                    dve.wait_ge(gram_ready, NB * t + b + 1)
                    copy_blocks(dve.tensor_copy, b, (3,), z_dve)
                    if not last:
                        make_one_hots(t + 1, 0, b, 2 * NB)

            make_one_hots(0, 0, 0, 2)
            macro_tiles(dve, body)

        @block.scalar
        def _(act):
            for i in range(NX):
                act.wait_ge(tab_loaded[i % STAGES], 16 * (i // STAGES + 1))
                act.copy(tab_hi[0:TP, i, :, :].rearrange("p c d -> p (c d)"), stage[i % STAGES]).then_inc(tab_hi_done, 1)

            def high_part(t, v):
                features = unit_features(SEQ[v])
                kind, n = SEQ[v]
                if kind == "oh":
                    act.wait_ge(oh_used, NCH * t + CH_AT[n + 1])
                else:
                    act.wait_ge(transposed, NJ * t + n + 1)
                act.copy(xh[:, :, span(features)],
                         x_bank(v, len(features)).rearrange("p (f b) -> p b f", b=MT)).then_inc(hi_done, 1)

            def layer_out(t, n):
                act.wait_ge(l_ready, NL * t + n + 1)
                ps = g_ps[:, n % 4, 0:MT]
                if n < 4:
                    act.activation(h1[:, n, :], ps, ACT.Relu, bias=b1_sb[:, n:n + 1]).then_inc(l_out, 1)
                elif n < 6:
                    act.activation(h2[:, n - 4, :], ps, ACT.Relu, bias=b2_sb[:, n - 4:n - 3]).then_inc(l_out, 1)
                else:
                    if not (isinstance(t, int) and t == 0):
                        act.wait_ge(y_stored, 16 * t)
                    act.copy(y[:, :], ps[0:1, :]).then_inc(l_out, 1)
                    act.wait_ge(l_out, NL * t + NL)
                    act.dma_start(out.rearrange("b o -> o b")[:, bass.ds(t * MT, MT)], y[:, :]).then_inc(y_stored, 16)

            def load_context(t):
                act.dma_start(z[96:96 + CTX, J - 1, :], ctx_t[:, bass.ds(t * MT, MT)]).then_inc(ctx_loaded, 16)

            def body(t, first, last):
                v = 0
                for u, units in STEPS:
                    high_part(t, v)
                    if not first and u < 4:
                        layer_out(t - 1, u)
                        if u == 3:
                            load_context(t)
                    for k in range(len(units)):
                        high_part(t, v + 1 + k)
                    v += 1 + len(units)
                for v in range(v, NU):
                    high_part(t, v)
                if not first:
                    for n in range(4, NL):
                        layer_out(t - 1, n)
                for b in range(NB):
                    act.wait_ge(gram_ready, NB * t + b + 1)
                    copy_blocks(act.copy, b, (0, 1, 2), z_act)

            act.wait_ge(pads_done, 2)
            load_context(0)
            act.wait_ge(w_loaded, 16 * 5)
            macro_tiles(act, body)
            for n in range(NL):
                layer_out(NM - 1, n)
            act.wait_ge(y_stored, 16 * NM)

        @block.tensor
        def _(pe):
            def broadcast_ids(t, u):
                if not (isinstance(t, int) and t == 0 and u < 2):
                    pe.wait_ge(oh_ready, NCH * t + (CH_AT[u - 1] if u >= 2 else CH_AT[NI - 1 + u] - NCH))
                    pe.nop(nofuse=True)
                for i in range(len(OH_UNITS[u])):
                    last = pe.matmul(ids_ps[:, u % 2, i * MT:(i + 1) * MT], sel[:, 2 * u + i, :],
                                     ids_f[:, bass.ds(t * MT, MT)], start=True, stop=True)
                last.then_inc(ids_bcast, 1)

            def x_bank_free(t, v):
                if not (isinstance(t, int) and t == 0 and v < 2):
                    pe.wait_ge(lo_done, NU * t + v - 1)

            def one_hot_unit(t, v, u):
                x_bank_free(t, v)
                for i, f in enumerate(OH_UNITS[u]):
                    dst = x_ps[:, v % 2, i * MT:(i + 1) * MT]
                    for c in range(TC):
                        at = CH_AT[u] + i * TC + c
                        pe.wait_ge(oh_ready, NCH * t + at + 1)
                        hot = one_hot[0:TP, at % OH_SLOTS, :]
                        pe.matmul(dst, tab_hi[0:TP, 2 * u + i, c, :], hot, start=(c == 0), stop=False)
                        last = pe.matmul(dst, tab_lo[0:TP, 2 * u + i, c, :], hot, start=False, stop=(c == TC - 1))
                        last.then_inc(oh_used, 1)

            def transpose_unit(t, v, j):
                x_bank_free(t, v)
                n = len(GA_UNITS[j]) * HALF
                pe.wait_ge(gathered[j], 16 * n * t + 16 * n)
                for i, f in enumerate(GA_UNITS[j]):
                    for h in range(HALF):
                        last = pe.transpose(x_ps[:, v % 2, (i * HALF + h) * P:(i * HALF + h + 1) * P],
                                            rows[:, GATHER.index(f), h, :], ident[:, :])
                last.then_inc(transposed, 1)

            def layer(t, n):
                dst = g_ps[:, n % 4, 0:MT]
                if n < 4:
                    if n == 0:
                        pe.wait_ge(z_act, NB * t + NB)
                        pe.wait_ge(z_dve, NB * t + NB)
                        pe.wait_ge(ctx_loaded, 16 * t + 16)
                    for j in range(J):
                        last = pe.matmul(dst, w1_sb[:, j, n * P:(n + 1) * P], z[:, j, :], start=(j == 0), stop=(j == J - 1))
                elif n < 6:
                    pe.wait_ge(l_out, NL * t + 4)
                    for k in range(H1 // P):
                        last = pe.matmul(dst, w2_sb[:, k, (n - 4) * P:(n - 3) * P], h1[:, k, :], start=(k == 0), stop=(k == H1 // P - 1))
                else:
                    pe.wait_ge(l_out, NL * t + 6)
                    for k in range(H2 // P):
                        last = pe.matmul(dst[0:1, :], w3_sb[:, k:k + 1], h2[:, k, :], start=(k == 0), stop=(k == H2 // P - 1))
                last.then_inc(l_ready, 1)

            def gram_batch(t, b):
                if not (isinstance(t, int) and t == 0 and b < 2):
                    pe.wait_ge(z_act, NB * t + b - 1)
                    pe.wait_ge(z_dve, NB * t + b - 1)
                for g in range(NG):
                    s0 = b * BS + 4 * g

                    hi, lo = (x[:, s0 * FS:(s0 + 4) * FS] for x in (x_hi, x_lo))
                    mhi, mlo = (x[:, s0:s0 + 4, 0:FM] for x in (xh, xl))
                    dst = g_ps[:, 2 * (b % 2) + g // 4, (g % 4) * 4 * FM:(g % 4 + 1) * 4 * FM]
                    pe.matmul(dst, hi, mhi, start=True, stop=False)
                    pe.matmul(dst, hi, mlo, start=False, stop=False)
                    last = pe.matmul(dst, lo, mhi, start=False, stop=True)
                last.then_inc(gram_ready, 1)

            def body(t, first, last):
                v = 0
                for u, units in STEPS:
                    if u + 1 < NI:
                        broadcast_ids(t, u + 1)
                    one_hot_unit(t, v, u)
                    if not first and u < 4:
                        layer(t - 1, u)
                    for k, j in enumerate(units):
                        transpose_unit(t, v + 1 + k, j)
                    v += 1 + len(units)
                for j in TAIL_UNITS:
                    transpose_unit(t, v, j)
                    v += 1
                if not last:
                    broadcast_ids(t + 1, 0)
                if not first:
                    for n in range(4, NL):
                        layer(t - 1, n)
                    pe.wait_ge(l_out, NL * t)
                pe.wait_ge(lo_done, NU * t + NU)
                for b in range(NB):
                    gram_batch(t, b)

            pe.wait_ge(ident_done, 1)
            pe.wait_ge(const_done, 2)
            pe.wait_ge(tab_lo_done, NX)
            broadcast_ids(0, 0)
            macro_tiles(pe, body)
            for n in range(NL):
                layer(NM - 1, n)


def w1_rows():
    at = np.full((4, 32, J), F * (F - 1) // 2 + CTX)
    for m in range(F):
        for n in range(m):
            at[m % 4, n, m // 4] = n * F - n * (n + 1) // 2 + m - n - 1
    at[3, 0:CTX, J - 1] = F * (F - 1) // 2 + np.arange(CTX)
    return at.reshape(P, J)


def kernel(**inputs):
    import concourse.bacc as bacc
    from concourse.bass_utils import run_bass_kernel_spmd as run

    nc = bacc.Bacc("TRN2", target_bir_lowering=False, num_devices=1)
    arrays = {}

    def given(name, a):
        a = np.ascontiguousarray(a)
        arrays["in_" + name] = a
        return nc.dram_tensor("in_" + name, a.shape, mybir.dt.from_np(a.dtype), kind="ExternalInput").ap()

    w1 = np.asarray(inputs["W_top1"])
    w1z = np.concatenate([w1, np.zeros((1, H1), w1.dtype)])[w1_rows()]
    ids = np.asarray(inputs["ids"])
    args = [given("ids", ids), given("ids_t", ids.T), given("ctx_t", np.asarray(inputs["dense_ctx"]).T),
            [given(f"tbl_{f}", inputs[f"tbl_{f}"]) for f in range(F)],
            given("w1z", w1z), given("b_top1", inputs["b_top1"]), given("W_top2", inputs["W_top2"]),
            given("b_top2", inputs["b_top2"]), given("W_top3", inputs["W_top3"])]
    out = nc.dram_tensor("out_0", (B, 1), F32, kind="ExternalOutput").ap()
    build(nc, *args, out)
    r = run(nc, [arrays], core_ids=[0])
    return r.results[0]["out_0"]
```

```python
from contextlib import ExitStack

import numpy as np

import concourse.bass as bass
from concourse import mybir

F32 = mybir.dt.float32
F32R = mybir.dt.float32r
I32 = mybir.dt.int32
ALU = mybir.AluOpType
ACT = mybir.ActivationFunctionType

B = 2048
F = 27
D = 128
CTX = 16
H1, H2 = 512, 256
P = 128
MT = 256
NM = B // MT
HALF = MT // P
FS = 32
FM = 28
J = FM // 4

ONE_HOT = (0, 2, 3, 6, 7, 11)
ROWS = 1000
TP = 125
TC = ROWS // TP
CG = 4
GT = TC // CG
GATHER = tuple(f for f in range(F) if f not in ONE_HOT)
NX = len(ONE_HOT)
OH_SLOTS = 4
STAGES = 3


def pairs(features):
    return [features[i:i + 2] for i in range(0, len(features), 2)]


OH_UNITS = pairs(ONE_HOT)
GA_UNITS = pairs(GATHER)
NI = len(OH_UNITS)
NJ = len(GA_UNITS)
PARTS = (range(0, NJ // 2), range(NJ // 2, NJ))
OG_AT = [GT * sum(len(u) for u in OH_UNITS[:n]) for n in range(NI + 1)]
NOG = OG_AT[NI]
assert NOG % OH_SLOTS == 0
NL = 7
NB = 8
BS = MT // NB
NG = BS // 4

ORDER = [("ids", 1), ("hot", 0), ("row", 0), ("row", 1), ("layer", 0),
         ("ids", 2), ("hot", 1), ("row", 2), ("layer", 1), ("row", 3), ("row", 4),
         ("hot", 2), ("row", 5), ("layer", 2), ("row", 6), ("row", 7), ("layer", 3),
         ("row", 8), ("layer", 4), ("row", 9), ("layer", 5), ("row", 10), ("layer", 6)]
UNITS = [w for w in ORDER if w[0] in ("hot", "row")]
NU = len(UNITS)
assert NU == NI + NJ and NU % 2 == 0


def known(t):
    return isinstance(t, int)


def build(nc, ids, ids_t, ctx_t, tables, w1z, b1, w2, b2, w3, out):
    ctx = ExitStack()
    with ctx:
        def sb(name, shape, dt=F32):
            return ctx.enter_context(nc.sbuf_tensor(name, shape, dt))

        def sem(name):
            return ctx.enter_context(nc.semaphore(name))

        ident = sb("ident", [P, P])
        row_of = sb("row_of", [P, TC])
        sel = sb("sel", [NX, NX, P], F32R)
        ids_rows = [sb(f"ids_rows{i}", [P, HALF, F], I32) for i in range(2)]
        ids_f = sb("ids_f", [NX, B], F32R)
        stage = sb("stage", [P, J * H1])
        tab_hi = sb("tab_hi", [P, NX, TC, D], F32R)
        tab_lo = sb("tab_lo", [P, NX, TC, D], F32R)
        one_hot = sb("one_hot", [P, OH_SLOTS, CG, MT], F32R)
        rows = sb("rows", [P, len(GATHER), HALF, D])
        x = sb("x", [P, MT, FS])
        z = sb("z", [P, J, MT])
        z_hi = sb("z_hi", [P, J, MT], F32R)
        z_lo = sb("z_lo", [P, J, MT], F32R)
        w1_hi = sb("w1_hi", [P, J, H1], F32R)
        w1_lo = sb("w1_lo", [P, J, H1], F32R)
        w2_sb = sb("w2_sb", [P, H1 // P, H2])
        w3_sb = sb("w3_sb", [P, H2 // P])
        b1_sb = sb("b1_sb", [P, H1 // P])
        b2_sb = sb("b2_sb", [P, H2 // P])
        h1 = sb("h1", [P, H1 // P, MT])
        h2 = sb("h2", [P, H2 // P, MT])
        y = sb("y", [1, MT])
        ids_ps = ctx.enter_context(nc.psum_tensor("ids_ps", [P, 2, 512], F32))
        x_ps = ctx.enter_context(nc.psum_tensor("x_ps", [P, 2, 512], F32))
        g_ps = ctx.enter_context(nc.psum_tensor("g_ps", [P, 4, 512], F32))

        ids_loaded = [sem(f"ids_loaded{i}") for i in range(2)]
        idsr_loaded = sem("idsr_loaded")
        tab_loaded = [sem(f"tab_loaded{i}") for i in range(STAGES)]
        tab_hi_done = sem("tab_hi_done")
        tab_lo_done = sem("tab_lo_done")
        w1_loaded = sem("w1_loaded")
        w1_hi_done = sem("w1_hi_done")
        w1_lo_done = sem("w1_lo_done")
        w_loaded = sem("w_loaded")
        ident_zero = sem("ident_zero")
        ident_done = sem("ident_done")
        row_done = sem("row_done")
        const_done = sem("const_done")
        pads_done = sem("pads_done")
        ids_bcast = sem("ids_bcast")
        oh_ready = sem("oh_ready")
        oh_used = sem("oh_used")
        gathered = [sem(f"gathered{j}") for j in range(NJ)]
        transposed = sem("transposed")
        x_out = sem("x_out")
        gram_ready = sem("gram_ready")
        z_act = sem("z_act")
        z_dve = sem("z_dve")
        z_hi_done = sem("z_hi_done")
        z_lo_done = sem("z_lo_done")
        ctx_loaded = sem("ctx_loaded")
        l_ready = sem("l_ready")
        l_out = sem("l_out")
        y_stored = sem("y_stored")

        stage_ids = stage[0:NX, 0:B].bitcast(I32)
        stage_tab = [stage[0:TP, i * TC * D:(i + 1) * TC * D] for i in range(STAGES)]
        assert STAGES * TC * D <= J * H1

        def flat(table):
            return table.rearrange("p c d -> p (c d)")

        def macro_tiles(engine, body):
            body(0, True, False)
            with engine.Fori(1, NM - 1) as t:
                body(t, False, False)
            body(NM - 1, False, True)

        def copy_blocks(copy, b, quadrants, signal):
            src = g_ps[:, 2 * (b % 2):2 * (b % 2) + 2, 0:4 * 4 * FM].rearrange("p a (g s j q) -> p a g s j q", g=4, s=4, q=4)
            dst = z[:, :, b * BS:(b + 1) * BS].rearrange("p j (a g s) -> p a g s j", g=4, s=4)
            for s in quadrants:
                for q in range(4):
                    nj = J - 1 if q == 3 else J
                    last = copy(dst[32 * q:32 * q + F, :, :, s, 0:nj], src[32 * s:32 * s + F, :, :, s, 0:nj, q])
            last.then_inc(signal, 1)

        block = ctx.enter_context(nc.Block())

        @block.sync
        def _(sp):
            def load_ids(t, part):
                sp.dma_start(ids_rows[part][:, :, :],
                             ids.rearrange("(c p) f -> p c f", p=P)[:, bass.ds(t * HALF, HALF), :]).then_inc(ids_loaded[part], 16)

            for part in range(2):
                load_ids(0, part)
            for i, f in enumerate(ONE_HOT):
                sp.dma_start(stage_ids[i:i + 1, :], ids_t[f:f + 1, :]).then_inc(idsr_loaded, 16)
            sp.wait_ge(const_done, 2)
            for i in range(NX):
                if i >= STAGES:
                    sp.wait_ge(tab_lo_done, i - STAGES + 1)
                sp.dma_start(stage_tab[i % STAGES],
                             tables[ONE_HOT[i]].rearrange("(p c) d -> p (c d)", c=TC)).then_inc(tab_loaded[i % STAGES], 16)
            sp.dma_start(w2_sb[:, :, :], w2.rearrange("(k p) n -> p k n", p=P)).then_inc(w_loaded, 16)
            with nc.allow_non_contiguous_dma(reason="biases and the last layer's weights, once"):
                sp.dma_start(w3_sb[:, :], w3.rearrange("(k p) n -> p (k n)", p=P)).then_inc(w_loaded, 16)
                sp.dma_start(b1_sb[:, :], b1.rearrange("(k p) -> p k", p=P)).then_inc(w_loaded, 16)
                sp.dma_start(b2_sb[:, :], b2.rearrange("(k p) -> p k", p=P)).then_inc(w_loaded, 16)
            sp.wait_ge(tab_lo_done, NX)
            sp.dma_start(stage[:, :], w1z.rearrange("p j k -> p (j k)")).then_inc(w1_loaded, 16)

            def body(t, first, last):
                for part, units in enumerate(PARTS):
                    for j in units:
                        sp.wait_ge(gathered[j], 16 * HALF * len(GA_UNITS[j]) * (t + 1))
                        sp.nop(nofuse=True)
                    load_ids(t + 1, part)

            body(0, True, False)
            with sp.Fori(1, NM - 1) as t:
                body(t, False, False)

        @block.gpsimd
        def _(pool):
            pool.memset(ident[:, :], 0.0).then_inc(ident_zero, 1)
            pool.wait_ge(ident_zero, 1)
            pool.affine_select(out=ident[:, :], in_=ident[:, :], compare_op=ALU.not_equal, fill=1.0,
                               base=0, pattern=[[-1, P]], channel_multiplier=1).then_inc(ident_done, 1)
            pool.iota(row_of[:, :], pattern=[[1, TC]], base=0, channel_multiplier=TC,
                      allow_small_or_imprecise_dtypes=True).then_inc(row_done, 1)

            def body(t, first, last):
                for j, unit in enumerate(GA_UNITS):
                    part = int(j in PARTS[1])
                    if j in (PARTS[0][0], PARTS[1][0]):
                        pool.wait_ge(ids_loaded[part], 16 * t + 16)
                        pool.nop(nofuse=True)
                    if not first:
                        pool.wait_ge(transposed, NJ * (t - 1) + j + 1)
                        pool.nop(nofuse=True)
                    for f in unit:
                        for h in range(HALF):
                            pool.indirect_dma_start(
                                out=rows[:, GATHER.index(f), h, :], out_offset=None, in_=tables[f][:, :],
                                in_offset=bass.IndirectOffsetOnAxis(
                                    ap=ids_rows[part][:, h, f:f + 1], axis=0),
                            ).then_inc(gathered[j], 16)

            macro_tiles(pool, body)

        @block.vector
        def _(dve):
            dve.memset(z[:, :, :], 0.0).then_inc(pads_done, 1)
            dve.memset(x[:, :, F:FS], 0.0).then_inc(pads_done, 1)
            dve.wait_ge(ident_done, 1)
            dve.tensor_copy(sel[:, :, :], ident[0:NX, 0:NX].unsqueeze(2).to_broadcast([NX, NX, P])).then_inc(const_done, 1)
            dve.wait_ge(idsr_loaded, 16 * NX)
            dve.tensor_copy(ids_f[:, :], stage_ids).then_inc(const_done, 1)
            for i in range(NX):
                dve.wait_ge(tab_hi_done, i + 1)
                dve.tensor_tensor(flat(tab_lo[0:TP, i, :, :]), stage_tab[i % STAGES],
                                  flat(tab_hi[0:TP, i, :, :]).bitcast(F32), ALU.subtract).then_inc(tab_lo_done, 1)
            dve.wait_ge(row_done, 1)

            def make_one_hots(t, u, groups):
                for n in groups:
                    at = OG_AT[u] + n
                    dve.wait_ge(ids_bcast, NI * t + u + 1)
                    if not (known(t) and t == 0 and at < OH_SLOTS):
                        dve.wait_ge(oh_used, NOG * t + at - OH_SLOTS + 1)
                    i, c = n // GT, n % GT * CG
                    dve.tensor_tensor(one_hot[0:TP, at % OH_SLOTS, :, :],
                                      ids_ps[0:TP, u % 2, i * MT:(i + 1) * MT].unsqueeze(1).to_broadcast([TP, CG, MT]),
                                      row_of[0:TP, c:c + CG].unsqueeze(2).to_broadcast([TP, CG, MT]),
                                      ALU.is_equal).then_inc(oh_ready, 1)

            def all_groups(u):
                return range(OG_AT[u + 1] - OG_AT[u])

            def split_z(t):
                dve.wait_ge(z_hi_done, t + 1)
                dve.tensor_tensor(flat(z_lo[:, :, :]), flat(z[:, :, :]), flat(z_hi[:, :, :]).bitcast(F32),
                                  ALU.subtract).then_inc(z_lo_done, 1)

            def body(t, first, last):
                if not first:
                    split_z(t - 1)
                for u in range(1, NI):
                    make_one_hots(t, u, all_groups(u))
                if first:
                    dve.wait_ge(w1_hi_done, 1)
                    dve.tensor_tensor(flat(w1_lo[:, :, :]), stage[:, :], flat(w1_hi[:, :, :]).bitcast(F32),
                                      ALU.subtract).then_inc(w1_lo_done, 1)
                for b in range(NB):
                    dve.wait_ge(gram_ready, NB * t + b + 1)
                    copy_blocks(dve.tensor_copy, b, (2, 3), z_dve)
                    if not last and b % 2 == 1:
                        make_one_hots(t + 1, 0, [b // 2])

            make_one_hots(0, 0, all_groups(0))
            macro_tiles(dve, body)
            split_z(NM - 1)

        @block.scalar
        def _(act):
            for i in range(NX):
                act.wait_ge(tab_loaded[i % STAGES], 16 * (i // STAGES + 1))
                act.copy(flat(tab_hi[0:TP, i, :, :]), stage_tab[i % STAGES]).then_inc(tab_hi_done, 1)

            def copy_x(t, v):
                kind, n = UNITS[v]
                if kind == "hot":
                    act.wait_ge(oh_used, NOG * t + OG_AT[n + 1])
                    unit = OH_UNITS[n]
                else:
                    act.wait_ge(transposed, NJ * t + n + 1)
                    unit = GA_UNITS[n]
                a, b = unit[0], unit[-1]
                act.copy(x[:, :, a:b + 1:max(b - a, 1)],
                         x_ps[:, v % 2, 0:len(unit) * MT].rearrange("p (f b) -> p b f", b=MT)).then_inc(x_out, 1)

            def layer_out(t, n):
                act.wait_ge(l_ready, NL * t + n + 1)
                ps = g_ps[:, n % 4, 0:MT]
                if n < 4:
                    act.activation(h1[:, n, :], ps, ACT.Relu, bias=b1_sb[:, n:n + 1]).then_inc(l_out, 1)
                elif n < 6:
                    act.activation(h2[:, n - 4, :], ps, ACT.Relu, bias=b2_sb[:, n - 4:n - 3]).then_inc(l_out, 1)
                else:
                    if not (known(t) and t == 0):
                        act.wait_ge(y_stored, 16 * t)
                    act.copy(y[:, :], ps[0:1, :]).then_inc(l_out, 1)
                    act.wait_ge(l_out, NL * t + NL)
                    act.dma_start(out.rearrange("b o -> o b")[:, bass.ds(t * MT, MT)], y[:, :]).then_inc(y_stored, 16)

            def load_context(t):
                act.dma_start(z[96:96 + CTX, J - 1, :], ctx_t[:, bass.ds(t * MT, MT)]).then_inc(ctx_loaded, 16)

            def split_z(t):
                act.wait_ge(z_act, NB * t + NB)
                act.wait_ge(z_dve, NB * t + NB)
                act.wait_ge(ctx_loaded, 16 * t + 16)
                act.copy(flat(z_hi[:, :, :]), flat(z[:, :, :])).then_inc(z_hi_done, 1)

            def body(t, first, last):
                if not first:
                    split_z(t - 1)
                v = 0
                for kind, n in ORDER:
                    if kind in ("hot", "row"):
                        copy_x(t, v)
                        v += 1
                    elif kind == "layer" and not first:
                        layer_out(t - 1, n)
                        if n == 0:
                            act.wait_ge(z_lo_done, t)
                            load_context(t)
                if first:
                    act.wait_ge(w1_loaded, 16)
                    act.copy(flat(w1_hi[:, :, :]), stage[:, :]).then_inc(w1_hi_done, 1)
                for b in range(NB):
                    act.wait_ge(gram_ready, NB * t + b + 1)
                    copy_blocks(act.copy, b, (0, 1), z_act)

            act.wait_ge(pads_done, 2)
            load_context(0)
            act.wait_ge(w_loaded, 16 * 4)
            macro_tiles(act, body)
            split_z(NM - 1)
            for n in range(NL):
                layer_out(NM - 1, n)
            act.wait_ge(y_stored, 16 * NM)

        @block.tensor
        def _(pe):
            def broadcast_ids(t, u):
                same_bank = [w for w in range(NI) if w % 2 == u % 2]
                before = same_bank[same_bank.index(u) - 1]
                if before < u:
                    pe.wait_ge(oh_ready, NOG * t + OG_AT[before + 1])
                elif not (known(t) and t == 0):
                    pe.wait_ge(oh_ready, NOG * (t - 1) + OG_AT[before + 1])
                pe.nop(nofuse=True)
                for i in range(len(OH_UNITS[u])):
                    last = pe.matmul(ids_ps[:, u % 2, i * MT:(i + 1) * MT], sel[:, 2 * u + i, :],
                                     ids_f[:, bass.ds(t * MT, MT)], start=True, stop=True)
                last.then_inc(ids_bcast, 1)

            def x_bank_free(t, v):
                if not (known(t) and t == 0 and v < 2):
                    pe.wait_ge(x_out, NU * t + v - 1)

            def hot_unit(t, v, u):
                x_bank_free(t, v)
                for i in range(len(OH_UNITS[u])):
                    dst = x_ps[:, v % 2, i * MT:(i + 1) * MT]
                    for c in range(TC):
                        at = OG_AT[u] + i * GT + c // CG
                        if c % CG == 0:
                            pe.wait_ge(oh_ready, NOG * t + at + 1)
                        hot = one_hot[0:TP, at % OH_SLOTS, c % CG, :]
                        pe.matmul(dst, tab_hi[0:TP, 2 * u + i, c, :], hot, start=(c == 0), stop=False)
                        last = pe.matmul(dst, tab_lo[0:TP, 2 * u + i, c, :], hot, start=False, stop=(c == TC - 1))
                        if c % CG == CG - 1:
                            last.then_inc(oh_used, 1)

            def row_unit(t, v, j):
                x_bank_free(t, v)
                n = len(GA_UNITS[j]) * HALF
                pe.wait_ge(gathered[j], 16 * n * t + 16 * n)
                for i, f in enumerate(GA_UNITS[j]):
                    for h in range(HALF):
                        last = pe.transpose(x_ps[:, v % 2, (i * HALF + h) * P:(i * HALF + h + 1) * P],
                                            rows[:, GATHER.index(f), h, :], ident[:, :])
                last.then_inc(transposed, 1)

            def layer(t, n):
                dst = g_ps[:, n % 4, 0:MT]
                if n < 4:
                    if n == 0:
                        pe.wait_ge(z_lo_done, t + 1)
                    cols = slice(n * P, (n + 1) * P)
                    for j in range(J):
                        pe.matmul(dst, w1_hi[:, j, cols], z_hi[:, j, :], start=(j == 0), stop=False)
                        pe.matmul(dst, w1_hi[:, j, cols], z_lo[:, j, :], start=False, stop=False)
                        last = pe.matmul(dst, w1_lo[:, j, cols], z_hi[:, j, :], start=False, stop=(j == J - 1))
                elif n < 6:
                    pe.wait_ge(l_out, NL * t + 4)
                    cols = slice((n - 4) * P, (n - 3) * P)
                    for k in range(H1 // P):
                        last = pe.matmul(dst, w2_sb[:, k, cols], h1[:, k, :], start=(k == 0), stop=(k == H1 // P - 1))
                else:
                    pe.wait_ge(l_out, NL * t + 6)
                    for k in range(H2 // P):
                        last = pe.matmul(dst[0:1, :], w3_sb[:, k:k + 1], h2[:, k, :], start=(k == 0), stop=(k == H2 // P - 1))
                last.then_inc(l_ready, 1)

            def gram_batch(t, b):
                if not (known(t) and t == 0 and b < 2):
                    pe.wait_ge(z_act, NB * t + b - 1)
                    pe.wait_ge(z_dve, NB * t + b - 1)
                for g in range(NG):
                    s0 = b * BS + 4 * g
                    last = pe.matmul(g_ps[:, 2 * (b % 2) + g // 4, (g % 4) * 4 * FM:(g % 4 + 1) * 4 * FM],
                                     x[:, s0:s0 + 4, :].rearrange("p b f -> p (b f)"), x[:, s0:s0 + 4, 0:FM],
                                     start=True, stop=True)
                last.then_inc(gram_ready, 1)

            def body(t, first, last):
                v = 0
                for kind, n in ORDER:
                    if kind == "ids":
                        broadcast_ids(t, n)
                    elif kind == "hot":
                        hot_unit(t, v, n)
                        v += 1
                    elif kind == "row":
                        row_unit(t, v, n)
                        v += 1
                    elif not first:
                        layer(t - 1, n)
                if not last:
                    broadcast_ids(t + 1, 0)
                pe.wait_ge(x_out, NU * t + NU)
                if not first:
                    pe.wait_ge(l_out, NL * t)
                for b in range(NB):
                    gram_batch(t, b)

            pe.wait_ge(ident_done, 1)
            pe.wait_ge(const_done, 2)
            broadcast_ids(0, 0)
            pe.wait_ge(tab_lo_done, NX)
            macro_tiles(pe, body)
            for n in range(NL):
                layer(NM - 1, n)


def w1_rows():
    at = np.full((4, 32, J), F * (F - 1) // 2 + CTX)
    for m in range(F):
        for n in range(m):
            at[m % 4, n, m // 4] = n * F - n * (n + 1) // 2 + m - n - 1
    at[3, 0:CTX, J - 1] = F * (F - 1) // 2 + np.arange(CTX)
    return at.reshape(P, J)


def kernel(**inputs):
    import concourse.bacc as bacc
    from concourse.bass_utils import run_bass_kernel_spmd as run

    nc = bacc.Bacc("TRN2", target_bir_lowering=False, num_devices=1)
    arrays = {}

    def given(name, a):
        a = np.ascontiguousarray(a)
        arrays["in_" + name] = a
        return nc.dram_tensor("in_" + name, a.shape, mybir.dt.from_np(a.dtype), kind="ExternalInput").ap()

    w1 = np.asarray(inputs["W_top1"])
    w1z = np.concatenate([w1, np.zeros((1, H1), w1.dtype)])[w1_rows()]
    ids = np.asarray(inputs["ids"])
    args = [given("ids", ids), given("ids_t", ids.T), given("ctx_t", np.asarray(inputs["dense_ctx"]).T),
            [given(f"tbl_{f}", inputs[f"tbl_{f}"]) for f in range(F)],
            given("w1z", w1z), given("b_top1", inputs["b_top1"]), given("W_top2", inputs["W_top2"]),
            given("b_top2", inputs["b_top2"]), given("W_top3", inputs["W_top3"])]
    out = nc.dram_tensor("out_0", (B, 1), F32, kind="ExternalOutput").ap()
    build(nc, *args, out)
    r = run(nc, [arrays], core_ids=[0])
    return r.results[0]["out_0"]
```

```python
from contextlib import ExitStack

import numpy as np

import concourse.bass as bass
from concourse import mybir

F32 = mybir.dt.float32
F32R = mybir.dt.float32r
I32 = mybir.dt.int32
ALU = mybir.AluOpType
ACT = mybir.ActivationFunctionType

B = 2048
F = 27
D = 128
CTX = 16
H1, H2 = 512, 256
P = 128
MT = 256
NM = B // MT
HALF = MT // P
FS = 32
J = 4
GROUPS = -(-F // J)

ONE_HOT = (11, 12, 20, 21, 22, 23, 25, 26)
ROWS = 1000
TP = 125
TC = ROWS // TP
UF = 2
CG = 2
GU = TC // CG
GATHER = tuple(f for f in range(F) if f not in ONE_HOT)
COLUMNS = GATHER + ONE_HOT
NX = len(ONE_HOT)
OH_SLOTS = 4
STAGES = 5
W1_STAGES = 2
OH_UNITS = [ONE_HOT[i:i + UF] for i in range(0, NX, UF)]
assert all(unit == tuple(range(unit[0], unit[0] + UF)) for unit in OH_UNITS)
QUADS = [GATHER[i:i + 4] for i in range(0, len(GATHER), 4)]
GA_UNITS = [(q, h) for h in range(HALF) for q in QUADS]
NI = len(OH_UNITS)
NJ = len(GA_UNITS)
PARTS = (range(0, len(QUADS)), range(len(QUADS), NJ))
NOG = GU * NI
assert NOG % OH_SLOTS == 0
NL = 7
NB = 8
BS = MT // NB
ZP = 4
NG = BS // 4

ORDER = [("ids", 1), ("split", 0), ("hot", 0), ("row", 0), ("ids", 2), ("row", 1), ("hot", 1),
         ("layer", 0), ("row", 2), ("layer", 1), ("ids", 3), ("hot", 2), ("row", 3), ("layer", 2),
         ("hot", 3), ("ids", NI), ("row", 4), ("layer", 3), ("gram", 0), ("row", 5), ("layer", 4),
         ("row", 6), ("gram", 1), ("row", 7), ("row", 8), ("gram", 2), ("row", 9), ("gram", 3),
         ("gram", 4), ("layer", 5), ("gram", 5), ("gram", 6), ("layer", 6), ("gram", 7)]
FIRST_ORDER = [("tables", 1), ("ids", 1), ("hot", 0), ("row", 0), ("row", 1), ("tables", 2), ("ids", 2), ("hot", 1),
               ("row", 2), ("tables", 3), ("ids", 3), ("hot", 2), ("row", 3),
               ("w1", 0), ("w1", 1), ("w1", 2), ("w1", 3), ("w2", 0), ("hot", 3), ("row", 4),
               ("gram", 0), ("gram", 1), ("row", 5), ("gram", 2), ("row", 6), ("gram", 3), ("row", 7),
               ("ids", NI), ("warm", 6), ("row", 8), ("warm", 12), ("row", 9), ("gram", 4), ("gram", 5),
               ("gram", 6), ("gram", 7)]
X_BANKS = 3
LATE = [("layer", 5), ("layer", 6)]
LAST_ORDER = [w for w in ORDER if w not in LATE] + LATE
UNITS = [w for w in ORDER if w[0] in ("hot", "row")]
NU = len(UNITS)
assert UNITS == [w for w in FIRST_ORDER if w[0] in ("hot", "row")]
assert NU == NI + NJ
FIRST_HALF = 1 + max(v for v, (kind, n) in enumerate(UNITS) if kind == "hot" or n in PARTS[0])


def cover():
    at = [[q] for q in range(4)]
    for r in range(1, GROUPS):
        for q in range(4):
            at[q].append((r + 3) % GROUPS if q == (r - 1) % 4 else at[q][-1])
    return at


def layers_of(at):
    ends = [r for r in range(GROUPS) if r == GROUPS - 1 or at[r] != at[r + 1]]
    return [(min((r + 1) * J, F), at[r]) for r in reversed(ends)]


assert GROUPS == 7
COVER = cover()
PAINT = [layers_of(COVER[q]) for q in range(4)]
LAYERS = max(len(layers) for layers in PAINT)
ACT_SAMPLES, DVE_SAMPLES = (0, 1), (2, 3)


def copies(b, t):
    return LAYERS * 2 * (NB * t + b)


def x_bank(v):
    kind, n = UNITS[v]
    return 0 if kind == "hot" else 1 + n % (X_BANKS - 1)


def known(t):
    return isinstance(t, int)


def build(nc, ids, ids_t, ctx_t, tables, w1z, b1, w2, b2, w3, out):
    ctx = ExitStack()
    with ctx:
        def sb(name, shape, dt=F32):
            return ctx.enter_context(nc.sbuf_tensor(name, shape, dt))

        def sem(name):
            return ctx.enter_context(nc.semaphore(name))

        ident = sb("ident", [P, P])
        row_of = sb("row_of", [P, TC])
        ids_rows = [sb(f"ids_rows{i}", [P, HALF, F], I32) for i in range(2)]
        ids_sb = sb("ids_sb", [P, NI, UF, MT], I32)
        stage = sb("stage", [P, STAGES * TC * D])
        tab_hi = sb("tab_hi", [P, NX, TC, D], F32R)
        tab_lo = sb("tab_lo", [P, NX, TC, D], F32R)
        one_hot = sb("one_hot", [P, OH_SLOTS, CG, UF * MT], F32R)
        rows = sb("rows", [P, NJ, 4, D])
        x = sb("x", [P, MT, FS])
        z = sb("z", [P, J, MT])
        z_hi = sb("z_hi", [P, J, MT], F32R)
        z_lo = sb("z_lo", [P, J, MT], F32R)
        w1_hi = sb("w1_hi", [P, J, H1], F32R)
        w1_lo = sb("w1_lo", [P, J, H1], F32R)
        w2_hi = sb("w2_hi", [P, H1 // P, H2], F32R)
        w2_lo = sb("w2_lo", [P, H1 // P, H2], F32R)
        w3_sb = sb("w3_sb", [P, H2 // P])
        b1_sb = sb("b1_sb", [P, H1 // P])
        b2_sb = sb("b2_sb", [P, H2 // P])
        h1 = stage[:, 0:H1 // P * MT].rearrange("p (k b) -> p k b", b=MT)
        h2 = stage[:, H1 // P * MT:(H1 + H2) // P * MT].rearrange("p (k b) -> p k b", b=MT)
        h1_hi = sb("h1_hi", [P, H1 // P, MT], F32R)
        h1_lo = sb("h1_lo", [P, H1 // P, MT], F32R)
        y = sb("y", [P, B // P])
        y_rows = sb("y_rows", [B // P, P])
        l_ps = ctx.enter_context(nc.psum_tensor("l_ps", [P, 512], F32))
        x_ps = ctx.enter_context(nc.psum_tensor("x_ps", [P, X_BANKS, 512], F32))
        g_ps = ctx.enter_context(nc.psum_tensor("g_ps", [P, 4, 512], F32))

        ids_loaded = [sem(f"ids_loaded{i}") for i in range(2)]
        hot_ids_loaded = [sem(f"hot_ids_loaded{u}") for u in range(NI)]
        tab_loaded = [sem(f"tab_loaded{i}") for i in range(STAGES)]
        tab_hi_done = sem("tab_hi_done")
        tab_lo_done = sem("tab_lo_done")
        w1_loaded = sem("w1_loaded")
        w1_hi_done = sem("w1_hi_done")
        w1_lo_done = sem("w1_lo_done")
        w2_loaded = sem("w2_loaded")
        w2_hi_done = sem("w2_hi_done")
        w2_lo_done = sem("w2_lo_done")
        w_loaded = sem("w_loaded")
        ident_zero = sem("ident_zero")
        ident_done = sem("ident_done")
        row_done = sem("row_done")
        pads_done = sem("pads_done")
        oh_ready = sem("oh_ready")
        oh_used = sem("oh_used")
        gathered = [sem(f"gathered{j}") for j in range(NJ)]
        transposed = sem("transposed")
        x_out = sem("x_out")
        gram_ready = sem("gram_ready")
        z_act = sem("z_act")
        z_dve = sem("z_dve")
        z_hi_done = sem("z_hi_done")
        z_lo_done = sem("z_lo_done")
        ctx_loaded = sem("ctx_loaded")
        l_ready = sem("l_ready")
        l_out = sem("l_out")
        h1_hi_done = sem("h1_hi_done")
        h1_lo_done = sem("h1_lo_done")
        y_turned = sem("y_turned")
        y_copied = sem("y_copied")
        y_stored = sem("y_stored")

        def stage_of(i):
            if i < STAGES:
                return i, -1
            return W1_STAGES + (i - STAGES), W1_STAGES + (i - STAGES)

        assert NX <= 2 * STAGES - W1_STAGES and J * H1 <= W1_STAGES * TC * D
        stage_tab = [stage[0:TP, stage_of(i)[0] * TC * D:(stage_of(i)[0] + 1) * TC * D] for i in range(NX)]
        stage_w1 = stage[:, 0:J * H1]
        stage_w2 = stage[:, W1_STAGES * TC * D:W1_STAGES * TC * D + H1 // P * H2]

        def flat(table):
            return table.rearrange("p c d -> p (c d)")

        def row_slots(j):
            features, h = GA_UNITS[j]
            return [(i, f, h) for i, f in enumerate(features)]

        def layer_ps(t, n):
            if n >= 4 and known(t) and t == NM - 1:
                return x_ps[:, n - 4, 0:MT if n < 6 else HALF]
            if n < 4:
                return g_ps[:, n, 0:MT]
            if n < 6:
                return l_ps[:, (n - 4) * MT:(n - 3) * MT]
            return l_ps[:, 0:HALF]

        def macro_tiles(engine, body):
            body(0, True, False)
            with engine.Fori(1, NM - 1) as t:
                body(t, False, False)
            body(NM - 1, False, True)

        def copy_blocks(engine, copy, t, b, samples, signal):
            src = g_ps[:, 2 * (b % 2):2 * (b % 2) + 2, 0:4 * 4 * F].rearrange("p a (g s m) -> p a g s m", g=4, s=4)
            dst = z[:, :, b * BS:(b + 1) * BS].rearrange("p j (a g s) -> p a g s j", g=4, s=4)
            for n, (k, s) in enumerate((k, s) for k in range(LAYERS) for s in samples):
                if k:
                    engine.wait_ge(signal, copies(b, t) + n - len(samples) + 1)
                for q in range(4):
                    if k < len(PAINT[q]):
                        nr, group = PAINT[q][k]
                        c, nj = group * J, min(J, F - group * J)
                        last = copy(dst[32 * q:32 * q + nr, :, :, s, 0:nj], src[32 * s:32 * s + nr, :, :, s, c:c + nj])
                last.then_inc(signal, 1)

        block = ctx.enter_context(nc.Block())

        @block.sync
        def _(sp):
            def load_ids(t, part):
                sp.dma_start(ids_rows[part][:, :, :],
                             ids.rearrange("(c p) f -> p c f", p=P)[:, bass.ds(t * HALF, HALF), :]).then_inc(ids_loaded[part], 16)

            def load_hot_ids(t, u):
                f = OH_UNITS[u][0]
                sp.dma_start(ids_sb[0:TP, u, :, :],
                             ids_t[f:f + UF, bass.ds(t * MT, MT)].unsqueeze(0).to_broadcast([TP, UF, MT])
                             ).then_inc(hot_ids_loaded[u], 16)

            load_ids(0, 0)
            load_hot_ids(0, 0)
            for i in range(NX):
                if i == 2:
                    load_hot_ids(0, 1)
                at, before = stage_of(i)
                if before >= 0:
                    sp.wait_ge(tab_lo_done, before + 1)
                sp.dma_start(stage_tab[i],
                             tables[ONE_HOT[i]].rearrange("(p c) d -> p (c d)", c=TC)).then_inc(tab_loaded[at], 16)
                if i == STAGES - 1:
                    load_ids(0, 1)
                    for u in range(2, NI):
                        load_hot_ids(0, u)
            with nc.allow_non_contiguous_dma(reason="biases and the last layer's weights, once"):
                sp.dma_start(w3_sb[:, :], w3.rearrange("(k p) n -> p (k n)", p=P)).then_inc(w_loaded, 16)
                sp.dma_start(b1_sb[:, :], b1.rearrange("(k p) -> p k", p=P)).then_inc(w_loaded, 16)
                sp.dma_start(b2_sb[:, :], b2.rearrange("(k p) -> p k", p=P)).then_inc(w_loaded, 16)
            sp.wait_ge(tab_lo_done, W1_STAGES + 1)
            sp.dma_start(stage_w1, w1z.rearrange("p j k -> p (j k)")).then_inc(w1_loaded, 16)
            sp.wait_ge(tab_lo_done, STAGES + 1)
            sp.dma_start(stage_w2.rearrange("p (k n) -> p k n", n=H2),
                         w2.rearrange("(k p) n -> p k n", p=P)).then_inc(w2_loaded, 16)

            def load_context(t):
                for q in range(4):
                    sp.dma_start(z[32 * q + F:32 * q + F + CTX // 4, 0, :],
                                 ctx_t[q * CTX // 4:(q + 1) * CTX // 4, bass.ds(t * MT, MT)]).then_inc(ctx_loaded, 16)

            def next_ids(t, part):
                for j in PARTS[part]:
                    sp.wait_ge(gathered[j], 16 * len(row_slots(j)) * (t + 1))
                    sp.nop(nofuse=True)
                load_ids(t + 1, part)

            def next_hot_ids(t, u):
                sp.wait_ge(oh_ready, NOG * t + GU * (u + 1))
                sp.nop(nofuse=True)
                load_hot_ids(t + 1, u)

            def body(t, first, last):
                if not last:
                    next_hot_ids(t, 0)
                    next_ids(t, 0)
                if first:
                    sp.wait_ge(pads_done, 1)
                else:
                    sp.wait_ge(z_lo_done, ZP * t)
                    sp.nop(nofuse=True)
                load_context(t)
                if not last:
                    next_hot_ids(t, 1)
                    next_hot_ids(t, 2)
                    next_ids(t, 1)
                    next_hot_ids(t, 3)

            macro_tiles(sp, body)

        @block.gpsimd
        def _(pool):
            pool.memset(ident[:, :], 0.0).then_inc(ident_zero, 1)
            pool.wait_ge(ident_zero, 1)
            pool.affine_select(out=ident[:, :], in_=ident[:, :], compare_op=ALU.not_equal, fill=1.0,
                               base=0, pattern=[[-1, P]], channel_multiplier=1).then_inc(ident_done, 1)
            pool.iota(row_of[:, :], pattern=[[1, TC]], base=0, channel_multiplier=TC,
                      allow_small_or_imprecise_dtypes=True).then_inc(row_done, 1)

            def body(t, first, last):
                for j in range(NJ):
                    part = int(j in PARTS[1])
                    if j in (PARTS[0][0], PARTS[1][0]):
                        pool.wait_ge(ids_loaded[part], 16 * t + 16)
                        pool.nop(nofuse=True)
                    if not first:
                        pool.wait_ge(transposed, NJ * (t - 1) + j + 1)
                        pool.nop(nofuse=True)
                    for i, f, h in row_slots(j):
                        pool.indirect_dma_start(
                            out=rows[:, j, i, :], out_offset=None, in_=tables[f][:, :],
                            in_offset=bass.IndirectOffsetOnAxis(ap=ids_rows[part][:, h, f:f + 1], axis=0),
                        ).then_inc(gathered[j], 16)

            macro_tiles(pool, body)

        @block.vector
        def _(dve):
            dve.memset(z[:, :, :], 0.0).then_inc(pads_done, 1)
            dve.memset(x[:, :, F:FS], 0.0).then_inc(pads_done, 1)
            dve.wait_ge(row_done, 1)

            def split_tables(u):
                for i in range(UF * u, UF * u + UF):
                    dve.wait_ge(tab_hi_done, i + 1)
                    dve.tensor_tensor(flat(tab_lo[0:TP, i, :, :]), stage_tab[i],
                                      flat(tab_hi[0:TP, i, :, :]).bitcast(F32), ALU.subtract).then_inc(tab_lo_done, 1)

            def make_one_hots(t, u):
                dve.wait_ge(hot_ids_loaded[u], 16 * t + 16)
                ids_u = ids_sb[0:TP, u, :, :].rearrange("p f b -> p (f b)")
                for g in range(GU):
                    at = GU * u + g
                    if not (known(t) and t == 0 and at < OH_SLOTS):
                        dve.wait_ge(oh_used, NOG * t + at - OH_SLOTS + 1)
                    for c in range(CG):
                        last = dve.tensor_scalar(one_hot[0:TP, at % OH_SLOTS, c, :], ids_u,
                                                 row_of[0:TP, g * CG + c:g * CG + c + 1], None, ALU.is_equal)
                    last.then_inc(oh_ready, 1)

            def split_z(t, part):
                dve.wait_ge(z_hi_done, ZP * t + part + 1)
                cols = slice(part * MT // ZP, (part + 1) * MT // ZP)
                dve.tensor_tensor(z_lo[:, :, cols], z[:, :, cols], z_hi[:, :, cols].bitcast(F32),
                                  ALU.subtract).then_inc(z_lo_done, 1)

            def split_h1(t, n):
                dve.wait_ge(h1_hi_done, 4 * t + n + 1)
                dve.tensor_tensor(h1_lo[:, n, :], h1[:, n, :], h1_hi[:, n, :].bitcast(F32),
                                  ALU.subtract).then_inc(h1_lo_done, 1)

            def body(t, first, last):
                for kind, n in FIRST_ORDER if first else LAST_ORDER if last else ORDER:
                    if kind == "tables":
                        split_tables(n)
                    elif kind == "ids" and n < NI:
                        make_one_hots(t, n)
                    elif kind == "split":
                        for part in range(ZP):
                            split_z(t - 1, part)
                    elif kind == "ids" and not last:
                        make_one_hots(t + 1, 0)
                    elif kind == "w1":
                        dve.wait_ge(w1_hi_done, n + 1)
                        dve.tensor_tensor(w1_lo[:, n, :], stage_w1[:, n * H1:(n + 1) * H1], w1_hi[:, n, :].bitcast(F32),
                                          ALU.subtract).then_inc(w1_lo_done, 1)
                    elif kind == "w2":
                        dve.wait_ge(w2_hi_done, 1)
                        dve.tensor_tensor(flat(w2_lo[:, :, :]), stage_w2, flat(w2_hi[:, :, :]).bitcast(F32),
                                          ALU.subtract).then_inc(w2_lo_done, 1)
                    elif kind == "layer" and n < 4:
                        split_h1(t - 1, n)
                    elif kind == "gram":
                        dve.wait_ge(gram_ready, NB * t + n + 1)
                        copy_blocks(dve, dve.tensor_copy, t, n, DVE_SAMPLES, z_dve)
                        if last and (n == NB - 1 or n and n % (NB // ZP) == 0):
                            split_z(t, (n + (n == NB - 1)) * ZP // NB - 1)

            make_one_hots(0, 0)
            split_tables(0)
            macro_tiles(dve, body)
            for n in range(4):
                split_h1(NM - 1, n)

        @block.scalar
        def _(act):
            def split_tables(u):
                for i in range(UF * u, UF * u + UF):
                    at, before = stage_of(i)
                    act.wait_ge(tab_loaded[at], 16 if before < 0 else 32)
                    act.copy(flat(tab_hi[0:TP, i, :, :]), stage_tab[i]).then_inc(tab_hi_done, 1)

            def copy_x(t, v):
                kind, n = UNITS[v]
                if kind == "hot":
                    act.wait_ge(oh_used, NOG * t + GU * (n + 1))
                    unit, s0, ns = OH_UNITS[n], 0, MT
                else:
                    act.wait_ge(transposed, NJ * t + n + 1)
                    unit, h = GA_UNITS[n]
                    s0, ns = h * P, P
                c = COLUMNS.index(unit[0])
                assert COLUMNS[c:c + len(unit)] == tuple(unit)
                act.copy(x[:, s0:s0 + ns, c:c + len(unit)],
                         x_ps[:, x_bank(v), 0:len(unit) * ns].rearrange("p (f b) -> p b f", b=ns)).then_inc(x_out, 1)

            def layer_out(t, n):
                if known(t) and t == 0 and n == 0:
                    act.wait_ge(w_loaded, 16 * 3)
                act.wait_ge(l_ready, NL * t + n + 1)
                ps = layer_ps(t, n)
                if n < 4:
                    act.activation(h1[:, n, :], ps, ACT.Relu, bias=b1_sb[:, n:n + 1]).then_inc(l_out, 1)
                    act.wait_ge(l_out, NL * t + n + 1)
                    act.copy(h1_hi[:, n, :], h1[:, n, :]).then_inc(h1_hi_done, 1)
                elif n < 6:
                    act.activation(h2[:, n - 4, :], ps, ACT.Relu, bias=b2_sb[:, n - 4:n - 3]).then_inc(l_out, 1)
                else:
                    act.copy(y[:, bass.ds(t * HALF, HALF)], ps).then_inc(l_out, 1)

            def split_z(t, part):
                act.wait_ge(z_act, copies((part + 1) * NB // ZP, t))
                act.wait_ge(z_dve, copies((part + 1) * NB // ZP, t))
                act.wait_ge(ctx_loaded, 16 * 4 * (t + 1))
                cols = slice(part * MT // ZP, (part + 1) * MT // ZP)
                act.copy(z_hi[:, :, cols], z[:, :, cols]).then_inc(z_hi_done, 1)

            def body(t, first, last):
                v = 0
                for kind, n in FIRST_ORDER if first else LAST_ORDER if last else ORDER:
                    if kind == "tables":
                        split_tables(n)
                    if kind in ("hot", "row"):
                        copy_x(t, v)
                        v += 1
                    elif kind == "layer":
                        layer_out(t - 1, n)
                    elif kind == "w1":
                        if n == 0:
                            act.wait_ge(w1_loaded, 16)
                        act.copy(w1_hi[:, n, :], stage_w1[:, n * H1:(n + 1) * H1]).then_inc(w1_hi_done, 1)
                    elif kind == "w2":
                        act.wait_ge(w2_loaded, 16)
                        act.copy(flat(w2_hi[:, :, :]), stage_w2).then_inc(w2_hi_done, 1)
                    elif kind == "split":
                        for part in range(ZP):
                            split_z(t - 1, part)
                    elif kind == "gram":
                        act.wait_ge(gram_ready, NB * t + n + 1)
                        copy_blocks(act, act.copy, t, n, ACT_SAMPLES, z_act)
                        if last and (n == NB - 1 or n and n % (NB // ZP) == 0):
                            split_z(t, (n + (n == NB - 1)) * ZP // NB - 1)

            split_tables(0)
            macro_tiles(act, body)
            for n in range(NL):
                layer_out(NM - 1, n)
            act.wait_ge(y_turned, 1)
            act.copy(y_rows[:, :], g_ps[0:B // P, 0, 0:P]).then_inc(y_copied, 1)
            act.wait_ge(y_copied, 1)
            act.dma_start(out.rearrange("(i p) o -> i (p o)", p=P), y_rows[:, :]).then_inc(y_stored, 16)
            act.wait_ge(y_stored, 16)

        @block.tensor
        def _(pe):
            def x_bank_free(t, v):
                users = [w for w in range(NU) if x_bank(w) == x_bank(v)]
                before = users[users.index(v) - 1]
                if before < v:
                    pe.wait_ge(x_out, NU * t + before + 1)
                elif not (known(t) and t == 0):
                    pe.wait_ge(x_out, NU * t - NU + before + 1)

            def hot_unit(t, v, u):
                x_bank_free(t, v)
                for i in range(UF):
                    if known(t) and t == 0:
                        pe.wait_ge(tab_lo_done, UF * u + i + 1)
                    dst = x_ps[:, x_bank(v), i * MT:(i + 1) * MT]
                    for c in range(TC):
                        at = GU * u + c // CG
                        if i == 0 and c % CG == 0:
                            pe.wait_ge(oh_ready, NOG * t + at + 1)
                        hot = one_hot[0:TP, at % OH_SLOTS, c % CG, i * MT:(i + 1) * MT]
                        pe.matmul(dst, tab_hi[0:TP, UF * u + i, c, :], hot, start=(c == 0), stop=False)
                        last = pe.matmul(dst, tab_lo[0:TP, UF * u + i, c, :], hot, start=False, stop=(c == TC - 1))
                        if i == UF - 1 and c % CG == CG - 1:
                            last.then_inc(oh_used, 1)

            def row_unit(t, v, j):
                x_bank_free(t, v)
                n = len(row_slots(j))
                pe.wait_ge(gathered[j], 16 * n * t + 16 * n)
                for i, _, _ in row_slots(j):
                    last = pe.transpose(x_ps[:, x_bank(v), i * P:(i + 1) * P], rows[:, j, i, :], ident[:, :])
                last.then_inc(transposed, 1)

            def layer(t, n):
                dst = layer_ps(t, n)
                if n < 4:
                    cols = slice(n * P, (n + 1) * P)
                    if n == 0:
                        pe.wait_ge(z_hi_done, ZP * t + ZP)
                    for j in range(J):
                        pe.matmul(dst, w1_hi[:, j, cols], z_hi[:, j, :], start=(j == 0), stop=False)
                    for j in range(J):
                        pe.matmul(dst, w1_lo[:, j, cols], z_hi[:, j, :], start=False, stop=False)
                    if n == 0:
                        pe.wait_ge(z_lo_done, ZP * t + ZP)
                    for j in range(J):
                        last = pe.matmul(dst, w1_hi[:, j, cols], z_lo[:, j, :], start=False, stop=(j == J - 1))
                elif n < 6:
                    cols = slice((n - 4) * P, (n - 3) * P)
                    if n == 5 and not (known(t) and t == NM - 1):
                        pe.wait_ge(l_out, NL * t + 5)
                    for k in range(H1 // P):
                        if n == 4:
                            pe.wait_ge(h1_hi_done, 4 * t + k + 1)
                        pe.matmul(dst, w2_hi[:, k, cols], h1_hi[:, k, :], start=(k == 0), stop=False)
                        pe.matmul(dst, w2_lo[:, k, cols], h1_hi[:, k, :], start=False, stop=False)
                    if n == 4:
                        pe.wait_ge(h1_lo_done, 4 * t + 4)
                    for k in range(H1 // P):
                        last = pe.matmul(dst, w2_hi[:, k, cols], h1_lo[:, k, :], start=False, stop=(k == H1 // P - 1))
                else:
                    pe.wait_ge(l_out, NL * t + 6)
                    for h in range(HALF):
                        for k in range(H2 // P):
                            last = pe.matmul(dst[:, h:h + 1], h2[:, k, h * P:(h + 1) * P], w3_sb[:, k:k + 1],
                                             start=(k == 0), stop=(k == H2 // P - 1))
                last.then_inc(l_ready, 1)

            def gram_batch(t, b):
                if not (known(t) and t == 0 and b < 2):
                    pe.wait_ge(z_act, copies(b - 1, t))
                    pe.wait_ge(z_dve, copies(b - 1, t))
                for g in range(NG):
                    s0 = b * BS + 4 * g
                    last = pe.matmul(g_ps[:, 2 * (b % 2) + g // 4, (g % 4) * 4 * F:(g % 4 + 1) * 4 * F],
                                     x[:, s0:s0 + 4, :].rearrange("p b f -> p (b f)"), x[:, s0:s0 + 4, 0:F],
                                     start=True, stop=True)
                last.then_inc(gram_ready, 1)

            def body(t, first, last):
                v = 0
                for kind, n in FIRST_ORDER if first else LAST_ORDER if last else ORDER:
                    if kind == "hot":
                        hot_unit(t, v, n)
                        v += 1
                    elif kind == "warm":
                        keep_warm(n)
                    elif kind == "row":
                        row_unit(t, v, n)
                        v += 1
                    elif kind == "gram":
                        if first and n == 0:
                            pe.wait_ge(pads_done, 2)
                        if n == 0:
                            pe.wait_ge(x_out, NU * t + FIRST_HALF)
                        elif n == NB // 2:
                            pe.wait_ge(x_out, NU * t + NU)
                        if not first and n < 2:
                            pe.wait_ge(l_out, NL * t - NL + 2 * n + 2)
                        gram_batch(t, n)
                    elif kind == "layer":
                        layer(t - 1, n)

            def keep_warm(products):
                for _ in range(products):
                    pe.matmul(l_ps[:, 0:P], ident[:, :], ident[:, :], start=True, stop=True)

            pe.wait_ge(ident_done, 1)
            keep_warm(12)
            macro_tiles(pe, body)
            for n in range(NL):
                layer(NM - 1, n)
            pe.wait_ge(l_out, NL * NM)
            pe.transpose(g_ps[0:B // P, 0, 0:P], y[:, :], ident[:, :]).then_inc(y_turned, 1)


def w1_rows():
    unused = F * (F - 1) // 2 + CTX
    at = np.full((4, 32, J), unused)
    for q in range(4):
        for n in range(F):
            group = COVER[q][n // J]
            for j in range(min(J, F - group * J)):
                m = group * J + j
                if group != n // J or n < m:
                    a, b = sorted((COLUMNS[n], COLUMNS[m]))
                    at[q, n, j] = a * F - a * (a + 1) // 2 + b - a - 1
        at[q, F:F + CTX // 4, 0] = F * (F - 1) // 2 + np.arange(q * CTX // 4, (q + 1) * CTX // 4)
    assert sorted(at[at < unused]) == list(range(unused))
    return at.reshape(P, J)


def kernel(**inputs):
    import concourse.bacc as bacc
    from concourse.bass_utils import run_bass_kernel_spmd as run

    nc = bacc.Bacc("TRN2", target_bir_lowering=False, num_devices=1)
    arrays = {}

    def given(name, a):
        a = np.ascontiguousarray(a)
        arrays["in_" + name] = a
        return nc.dram_tensor("in_" + name, a.shape, mybir.dt.from_np(a.dtype), kind="ExternalInput").ap()

    w1 = np.asarray(inputs["W_top1"])
    w1z = np.concatenate([w1, np.zeros((1, H1), w1.dtype)])[w1_rows()]
    ids = np.asarray(inputs["ids"])
    args = [given("ids", ids), given("ids_t", ids.T), given("ctx_t", np.asarray(inputs["dense_ctx"]).T),
            [given(f"tbl_{f}", inputs[f"tbl_{f}"]) for f in range(F)],
            given("w1z", w1z), given("b_top1", inputs["b_top1"]), given("W_top2", inputs["W_top2"]),
            given("b_top2", inputs["b_top2"]), given("W_top3", inputs["W_top3"])]
    out = nc.dram_tensor("out_0", (B, 1), F32, kind="ExternalOutput").ap()
    build(nc, *args, out)
    r = run(nc, [arrays], core_ids=[0])
    return r.results[0]["out_0"]
```
